# Optimizing a Trainium2 kernel written in Bass

```python
import numpy as np
import jax
import jax.numpy as jnp

def _softmax(x, axis=-1):
    return jax.nn.softmax(x, axis=axis)

def _gelu(x):
    return jax.nn.gelu(x, approximate=True)

def _silu(x):
    return jax.nn.silu(x)

def _sigmoid(x):
    return jax.nn.sigmoid(x)

def _layernorm(x, axis=-1, eps=1e-05):
    m = jnp.mean(x, axis=axis, keepdims=True)
    v = jnp.var(x, axis=axis, keepdims=True)
    return (x - m) / jnp.sqrt(v + eps)

def _scatter_add(tgt, idx, src, axis=0):
    return tgt.at[idx].add(src)

def _segment_sum(src, seg, n):
    return jax.ops.segment_sum(src, seg, n)
kernel_name = 'mk_adaln_ffn_d1_seqx_r8_dcd929'

def setup_inputs(seed: int=0):
    np.random.seed(seed)
    _w = jnp.asarray

    def _rec_inputs():
        import jax
        import jax.numpy as jnp
        _rk = jax.random.key(seed)
        x = -1.394e-06 + 0.9999 * jax.random.normal(jax.random.fold_in(_rk, 1), (32, 32, 256), jnp.float32)
        _lenS = 32 - jax.random.randint(jax.random.fold_in(_rk, 7), (32,), 0, max(1, 32 // 4) + 1, jnp.int32)
        _lenS2 = 32 - jax.random.randint(jax.random.fold_in(_rk, 8), (32,), 0, max(1, 32 // 4) + 1, jnp.int32)
        cond_2048 = -0.00499425 + 1.0058 * jax.random.normal(jax.random.fold_in(_rk, 11), (32, 256), jnp.float32)
        return (x, cond_2048)
    x, cond_2048 = _rec_inputs()

    def _L0_cond_setup():
        import jax, jax.numpy as jnp
        import numpy as np
        B, T, D = (16, 128, 256)
        key = jax.random.key(seed)
        k0, k1, k2, k3 = jax.random.split(key, 4)
        scale = 1.0 / np.sqrt(D)
        return {'initial_state': jax.random.normal(k0, (B, D), jnp.float32), 'inputs': jax.random.normal(k1, (B, T, D), jnp.float32), 'W_ih': jax.random.normal(k2, (D, 3 * D), jnp.float32) * scale, 'W_hh': jax.random.normal(k3, (D, 3 * D), jnp.float32) * scale, 'b_ih': jnp.zeros((3 * D,), jnp.float32), 'b_hh': jnp.zeros((3 * D,), jnp.float32)}
    _L0_cond_all = _L0_cond_setup()
    _L0_cond_in = {k: v for k, v in _L0_cond_all.items() if k in ('W_ih', 'W_hh', 'b_ih', 'b_hh')}
    del _L0_cond_all

    def _L0_ffn_setup():
        import jax, jax.numpy as jnp
        import numpy as np
        B, S, D_IN, D_OUT = (4, 256, 256, 256)
        EPS = 1e-10
        key = jax.random.key(seed)
        kx, kw, kb = jax.random.split(key, 3)
        x = jax.random.normal(kx, (B, S, D_IN), dtype=jnp.float32)
        weight = jax.random.normal(kw, (D_OUT, D_IN), dtype=jnp.float32) * 0.02
        bias = jax.random.normal(kb, (D_OUT,), dtype=jnp.float32) * 0.02
        return {'x': x, 'weight': weight, 'bias': bias}
    _L0_ffn_all = _L0_ffn_setup()
    _L0_ffn_in = {k: v for k, v in _L0_ffn_all.items() if k in ('weight', 'bias')}
    del _L0_ffn_all
    return {'x': x, 'cond_2048': cond_2048, 'L0_cond_W_ih': _L0_cond_in['W_ih'], 'L0_cond_W_hh': _L0_cond_in['W_hh'], 'L0_cond_b_ih': _L0_cond_in['b_ih'], 'L0_cond_b_hh': _L0_cond_in['b_hh'], 'L0_ffn_weight': _L0_ffn_in['weight'], 'L0_ffn_bias': _L0_ffn_in['bias']}

def reference(x, cond_2048, L0_cond_W_ih, L0_cond_W_hh, L0_cond_b_ih, L0_cond_b_hh, L0_ffn_weight, L0_ffn_bias):
    import jax
    import jax.numpy as jnp

    def _L0_cond_ref(initial_state, inputs, W_ih, W_hh, b_ih, b_hh):
        import jax, jax.numpy as jnp
        import numpy as np
        B, T, D = (16, 128, 256)
        "ScanOverTime(GRU cell): sequential per-timestep module call with\n            dict-state passing; merge_dict_trees stacks the per-step\n            'state_predicted' tensors along axis=1 -> [B, T, D]."

        def cell(h, x):
            gi = x @ W_ih + b_ih
            gh = h @ W_hh + b_hh
            i_r, i_z, i_n = jnp.split(gi, 3, axis=-1)
            h_r, h_z, h_n = jnp.split(gh, 3, axis=-1)
            r = jax.nn.sigmoid(i_r + h_r)
            z = jax.nn.sigmoid(i_z + h_z)
            n = jnp.tanh(i_n + r * h_n)
            h_new = (1.0 - z) * n + z * h
            return (h_new, h_new)
        xs = jnp.swapaxes(inputs, 0, 1)
        _, hs = jax.lax.scan(cell, initial_state, xs)
        return jnp.swapaxes(hs, 0, 1)

    def _L0_ffn_ref(x, weight, bias):
        import jax, jax.numpy as jnp
        import numpy as np
        B, S, D_IN, D_OUT = (4, 256, 256, 256)
        EPS = 1e-10
        scale = jnp.mean(jnp.abs(weight))
        w_t = jnp.clip(jnp.round(weight / (scale + EPS)), -1.0, 1.0)
        w_ste = weight + jax.lax.stop_gradient(w_t * scale - weight)
        return jnp.einsum('bsi,oi->bso', x, w_ste) + bias
    x = x + _L0_ffn_ref(_L0_cond_ref(cond_2048, x, L0_cond_W_ih, L0_cond_W_hh, L0_cond_b_ih, L0_cond_b_hh), L0_ffn_weight, L0_ffn_bias)
    return x

_drawn_inputs = setup_inputs


def setup_inputs(seed=0):
    import zlib

    import numpy as np

    out = dict(_drawn_inputs(seed))
    spreads = {'L0_cond_b_ih': (0.0, 0.558), 'L0_cond_b_hh': (0.0, 0.8)}
    factors = {'L0_ffn_bias': 2.782}
    for name, (base, spread) in spreads.items():
        noise = np.random.default_rng([zlib.crc32(name.encode()), seed]).standard_normal(out[name].shape)
        drawn = base * np.exp(spread * noise) if base else spread * noise
        out[name] = jnp.asarray(drawn.astype(out[name].dtype))
    for name, factor in factors.items():
        out[name] = (out[name] * factor).astype(out[name].dtype)
    return out
```

```python
from contextlib import ExitStack

import concourse.bass as bass
from concourse import mybir

F32 = mybir.dt.float32
ALU = mybir.AluOpType
ACT = mybir.ActivationFunctionType
AX = mybir.AxisListType

P = 128
B, T, D = 32, 32, 256
BLOCKS = P // B
BW = D // BLOCKS
HALVES = 2
HW = BW // HALVES
GROUP = BLOCKS
GROUPS = T // GROUP
RING = 2 * GROUP
EPS = 1e-10
LOOPS = T // RING - 2
WT_STEPS = 9


def gru_projection_kernel(nc, x, h0, w_ih, w_hh, b_ih, b_hh, w_out, b_out, out):
    x_packed = x.rearrange("b t (j e) -> j b t e", j=BLOCKS)
    x_rows = x.rearrange("b t d -> t b d")
    out_rows = out.rearrange("b t d -> t b d")
    h0_packed = h0.rearrange("b (j e) -> j b e", j=BLOCKS)
    w_ih_rows = w_ih.rearrange("(j c d) n -> c j d n", j=BLOCKS, c=HALVES)
    w_hh_rows = w_hh.rearrange("(j c d) n -> c j d n", j=BLOCKS, c=HALVES)
    w_out_packed = w_out.rearrange("(q o) (j e) -> j o q e", o=B, j=BLOCKS)
    R, Z, N = 0, 1, 2

    def bias_rows(b, gate):
        return b[gate * D:(gate + 1) * D].rearrange("(j a e) -> j a e", j=BLOCKS, a=1).to_broadcast([BLOCKS, B, BW])

    with ExitStack() as ctx:
        def sb(name, shape):
            return ctx.enter_context(nc.sbuf_tensor(name, shape, F32))

        def pb(name, width):
            return ctx.enter_context(nc.psum_tensor(name, [P, 512], F32))[:, 0:width]

        def sem(name):
            return ctx.enter_context(nc.semaphore(name))

        wi = sb("wi", [P, HALVES, 3 * D])
        wh = sb("wh", [P, HALVES, 3 * D])
        wo = sb("wo", [P, D // B, BW])
        wt = sb("wt", [P, D // B, HALVES, B])
        w_pos = sb("w_pos", [P, D // B, HALVES, B])
        w_neg = sb("w_neg", [P, D // B, HALVES, B])
        w_abs = sb("w_abs", [P, D // B, BW])
        x_in = sb("x_in", [P, RING, BW])
        xT = sb("xT", [P, GROUP, HALVES, B])
        x_res = sb("x_res", [P, 2, D])
        y = sb("y", [P, 2, D])
        h = sb("h", [P, BW])
        hT = sb("hT", [P, HALVES, RING, B])
        gate_bias = sb("gate_bias", [P, 4, BW])
        bias_hh = sb("bias_hh", [P, 2, BW])
        out_bias = sb("out_bias", [P, D])
        zeros = sb("zeros", [P, D])
        ones = sb("ones", [P, P])
        r = sb("r", [P, BW])
        z = sb("z", [P, BW])
        u = sb("u", [P, BW])
        n = sb("n", [P, BW])
        rhn = sb("rhn", [P, BW])
        n_in = sb("n_in", [P, BW])
        n_pre = sb("n_pre", [P, BW])
        zh = sb("zh", [P, BW])
        un = sb("un", [P, BW])
        abs_sum = sb("abs_sum", [P, 1])
        scale = sb("scale", [P, 1])
        above = sb("above", [P, 1])
        below = sb("below", [P, 1])

        ps_rh = [pb(f"ps_rh{i}", 2 * BW) for i in range(2)]
        ps_zi = [pb(f"ps_zi{i}", 2 * BW) for i in range(2)]
        ps_y = [pb(f"ps_y{i}", D) for i in range(2)]
        ps_sum = pb("ps_sum", 1)

        s_x = [sem(f"s_x{i}") for i in range(2)]
        s_res = [sem(f"s_res{i}") for i in range(2)]
        s_wi = sem("s_wi")
        s_wh = sem("s_wh")
        s_wo = sem("s_wo")
        s_h0 = sem("s_h0")
        s_bias = sem("s_bias")
        s_obias = sem("s_obias")
        s_stored = sem("s_stored")
        s_const = sem("s_const")
        s_flags = sem("s_flags")
        s_gbias = sem("s_gbias")
        s_xT = sem("s_xT")
        s_seed = sem("s_seed")
        s_yseed = sem("s_yseed")
        s_rh = sem("s_rh")
        s_zi = sem("s_zi")
        s_gi = sem("s_gi")
        s_nin = sem("s_nin")
        s_r = sem("s_r")
        s_z = sem("s_z")
        s_u = sem("s_u")
        s_n = sem("s_n")
        s_rhn = sem("s_rhn")
        s_npre = sem("s_npre")
        s_zh = sem("s_zh")
        s_un = sem("s_un")
        s_h = sem("s_h")
        s_hT = sem("s_hT")
        s_yp = sem("s_yp")
        s_y = sem("s_y")
        s_wt = sem("s_wt")
        s_abs = sem("s_abs")
        s_sum = sem("s_sum")

        block = ctx.enter_context(nc.Block())

        @block.sync
        def _(sp):
            def load_x(g, slot):
                for j in range(BLOCKS):
                    sp.dma_start(x_in[j * B:(j + 1) * B, slot * GROUP:(slot + 1) * GROUP, :],
                                 x_packed[j, :, bass.ds(g * GROUP, GROUP), :]).then_inc(s_x[slot], 16)

            def load_residual(g, slot):
                sp.dma_start(x_res[:, slot, :], x_rows[bass.ds(g * GROUP, GROUP)]).then_inc(s_res[slot], 16)

            def store(g, slot):
                sp.dma_start(out_rows[bass.ds(g * GROUP, GROUP)], y[:, slot, :]).then_inc(s_stored, 16)

            load_x(0, 0)
            for c in range(HALVES):
                sp.dma_start(wi[:, c, :], w_ih_rows[c]).then_inc(s_wi, 16)
            for c in range(HALVES):
                sp.dma_start(wh[:, c, :], w_hh_rows[c]).then_inc(s_wh, 16)
            for j in range(BLOCKS):
                sp.dma_start(wo[j * B:(j + 1) * B], w_out_packed[j]).then_inc(s_wo, 16)
            load_x(1, 1)
            for g in range(2):
                load_residual(g, g)
                sp.wait_ge(s_xT, (g + 1) * GROUP)
                load_x(g + 2, g)

            def period(g, slot):
                sp.wait_ge(s_y, g - 1)
                store(g - 2, slot)
                if g_loads_x:
                    sp.wait_ge(s_xT, (g + 1) * GROUP)
                    load_x(g + 2, slot)
                sp.wait_ge(s_stored, 16 * (g - 1))
                load_residual(g, slot)

            g_loads_x = True
            with sp.Fori(1, GROUPS // 2 - 1) as i:
                for slot in range(2):
                    period(2 * i + slot, slot)
            g_loads_x = False
            for slot in range(2):
                period(GROUPS - 2 + slot, slot)
            for slot in range(2):
                sp.wait_ge(s_y, GROUPS - 2 + slot + 1)
                store(GROUPS - 2 + slot, slot)
            sp.wait_ge(s_stored, 16 * GROUPS)

        @block.gpsimd
        def _(pool):
            for part, (b, gate) in enumerate([(b_ih, R), (b_hh, N), (b_ih, Z), (b_ih, N)]):
                pool.dma_start(gate_bias[:, part, :], bias_rows(b, gate)).then_inc(s_bias, 16)
            for part, gate in enumerate([R, Z]):
                pool.dma_start(bias_hh[:, part, :], bias_rows(b_hh, gate)).then_inc(s_bias, 16)
            pool.dma_start(out_bias[:, :], b_out.rearrange("(a o) -> a o", a=1).to_broadcast([P, D])).then_inc(s_obias, 16)

        @block.scalar
        def _(act):
            act.dma_start(h[:, :], h0_packed).then_inc(s_h0, 16)

            def seed(s):
                act.activation(ps_zi[s % 2], gate_bias[:, 2:4, :].rearrange("p g e -> p (g e)"), ACT.Copy).then_inc(s_seed, 1)
                act.activation(ps_rh[s % 2], gate_bias[:, 0:2, :].rearrange("p g e -> p (g e)"), ACT.Copy).then_inc(s_seed, 1)

            def seed_y(slot):
                act.activation(ps_y[slot], out_bias[:, :], ACT.Copy).then_inc(s_yseed, 1)

            def step(t, s):
                last = isinstance(t, int) and t == T - 1
                if s % GROUP == 0 and not (isinstance(t, int) and t < GROUP):
                    seed_y((s // GROUP + 1) % 2)
                if not last:
                    if not (isinstance(t, int) and t == 0):
                        act.wait_ge(s_u, t)
                    seed(s + 1)
                act.wait_ge(s_rh, t + 1)
                act.activation(r[:, :], ps_rh[s % 2][:, 0:BW], ACT.Sigmoid).then_inc(s_r, 1)
                act.wait_ge(s_zi, t + 1)
                act.activation(z[:, :], ps_zi[s % 2][:, 0:BW], ACT.Sigmoid).then_inc(s_z, 1)
                act.activation(u[:, :], ps_zi[s % 2][:, 0:BW], ACT.Sigmoid, scale=-1.0).then_inc(s_u, 1)
                for c in range(HALVES):
                    act.wait_ge(s_npre, HALVES * t + c + 1)
                    act.activation(n[:, c * HW:(c + 1) * HW], n_pre[:, c * HW:(c + 1) * HW],
                                   ACT.Tanh).then_inc(s_n, 1)

            act.wait_ge(s_gbias, 1)
            act.wait_ge(s_flags, 1)
            seed(0)
            act.wait_ge(s_wo, 16 * BLOCKS)
            act.activation(w_abs[:, :, :], wo[:, :, :], ACT.Abs, accum_out=abs_sum[:, :]).then_inc(s_abs, 1)
            act.wait_ge(s_obias, 16)
            for t in range(RING):
                step(t, t)
            with act.Fori(1, LOOPS + 1) as i:
                for k in range(RING):
                    step(RING * i + k, k)
            for t in range(T - RING, T):
                step(t, t % RING)
            seed_y((GROUPS - 1) % 2)

        @block.tensor
        def _(pe):
            def tiles(bank, c0, stationary, moving):
                for j in range(BLOCKS):
                    mov = moving(j)
                    width = mov.shape[1] if len(mov.shape) == 2 else mov.shape[1] * mov.shape[2]
                    done = pe.matmul(bank[j * B:(j + 1) * B, c0:c0 + width], stationary, mov,
                                     start=False, stop=True, tile_position=(0, j * B), skip_group_check=True)
                return done

            def gates(w, c, first, count, stride=1):
                v = w[:, c, :].rearrange("p (g j e) -> p j g e", g=3, j=BLOCKS)
                return lambda j: v[:, j, first:first + stride * (count - 1) + 1:stride, :]

            def inputs_product(t, s):
                pe.wait_ge(s_xT, t + 1)
                pe.wait_ge(s_seed, 2 * (t + 1))
                for c in range(HALVES):
                    done = tiles(ps_zi[s % 2], 0, xT[:, s % GROUP, c, :], gates(wi, c, Z, 2))
                done.then_inc(s_gi, 1)
                for c in range(HALVES):
                    tiles(ps_rh[s % 2], 0, xT[:, s % GROUP, c, :], gates(wi, c, R, 1))

            def hidden_product(t, s):
                for c in range(HALVES):
                    pe.wait_ge(s_hT, HALVES * t + c + 1)
                    done = tiles(ps_rh[s % 2], 0, hT[:, c, s % RING, :], gates(wh, c, R, 2, N - R))
                done.then_inc(s_rh, 1)
                pe.wait_ge(s_nin, t + 1)
                for c in range(HALVES):
                    done = tiles(ps_zi[s % 2], 0, hT[:, c, s % RING, :], gates(wh, c, Z, 1))
                done.then_inc(s_zi, 1)

            def project(slot, piece, steps=range(GROUP)):
                c, half = piece % HALVES, piece // HALVES
                width = D // 2
                v = wt[:, :, c, :][:, half * width // B:(half + 1) * width // B, :]
                for q in steps:
                    ring = (slot * GROUP + q + 1) % RING
                    done = pe.matmul(ps_y[slot][q * B:(q + 1) * B, half * width:(half + 1) * width],
                                     hT[:, c, ring, :], v, start=False, stop=True,
                                     tile_position=(0, q * B), skip_group_check=True)
                return done

            def step(t, s, g):
                hidden_product(t, s)
                if not (isinstance(t, int) and t == T - 1):
                    inputs_product(t + 1, s + 1)
                if not (isinstance(t, int) and t < GROUP):
                    piece = s % GROUP
                    if piece == 0:
                        pe.wait_ge(s_yseed, g)
                        if isinstance(t, int) and t == GROUP:
                            pe.wait_ge(s_wt, WT_STEPS)
                    done = project((s // GROUP + 1) % 2, piece)
                    if piece == GROUP - 1:
                        done.then_inc(s_yp, 1)

            pe.wait_ge(s_const, 2)
            for bank in ps_rh + ps_zi + ps_y:
                for j in range(BLOCKS):
                    done = pe.matmul(bank[j * B:(j + 1) * B, :], zeros[:, 0:B], zeros[:, 0:bank.shape[1]],
                                     start=True, stop=True, tile_position=(0, j * B))
            done.then_inc(s_flags, 1)
            pe.wait_ge(s_wi, 16 * HALVES)
            inputs_product(0, 0)
            pe.wait_ge(s_wh, 16 * HALVES)
            for t in range(RING):
                step(t, t, t // GROUP)
                if t == 0:
                    pe.wait_ge(s_abs, 1)
                    pe.matmul(ps_sum, ones[:, :], abs_sum[:, :], start=True, stop=True).then_inc(s_sum, 1)
            with pe.Fori(1, LOOPS + 1) as i:
                for k in range(RING):
                    step(RING * i + k, k, 2 * i + k // GROUP)
            for t in range(T - RING, T):
                step(t, t % RING, t // GROUP)
            pe.wait_ge(s_yseed, GROUPS)
            for c in range(HALVES):
                pe.wait_ge(s_hT, HALVES * T + c + 1)
                for half in range(2):
                    done = project((GROUPS - 1) % 2, 2 * half + c)
            done.then_inc(s_yp, 1)

        @block.vector
        def _(dve):
            def transpose_x(s):
                dve.transpose(xT[:, s % GROUP, :, :].rearrange("p c b -> p (c b)"), x_in[:, s % RING, :]).then_inc(s_xT, 1)

            def read_out(g, rounds, slot):
                dve.wait_ge(s_yp, g + 1)
                dve.wait_ge(s_res[slot], 16 * (rounds + 1))
                dve.tensor_tensor(y[:, slot, :], ps_y[slot], x_res[:, slot, :], ALU.add).then_inc(s_y, 1)

            def step(t, s, rounds):
                g = 2 * rounds + s // GROUP
                last_steps = isinstance(t, int) and t >= T - 2
                if not last_steps:
                    if s % GROUP == GROUP - 2:
                        ahead = s // GROUP + 1
                        dve.wait_ge(s_x[ahead % 2], 16 * BLOCKS * (rounds + ahead // 2 + 1))
                    transpose_x(s + 2)
                if s % GROUP == 0 and not (isinstance(t, int) and t < RING):
                    read_out(g - 2, rounds - 1, s // GROUP)
                dve.wait_ge(s_gi, t + 1)
                dve.tensor_copy(n_in[:, :], ps_zi[s % 2][:, BW:2 * BW]).then_inc(s_nin, 1)
                half = [slice(c * HW, (c + 1) * HW) for c in range(HALVES)]
                dve.wait_ge(s_r, t + 1)
                for c in range(HALVES):
                    dve.tensor_tensor(rhn[:, half[c]], ps_rh[s % 2][:, BW + c * HW:BW + (c + 1) * HW], r[:, half[c]],
                                      ALU.mult).then_inc(s_rhn, 1)
                for c in range(HALVES):
                    dve.wait_ge(s_rhn, HALVES * t + c + 1)
                    if c == 0:
                        dve.wait_ge(s_nin, t + 1)
                    dve.tensor_tensor(n_pre[:, half[c]], n_in[:, half[c]], rhn[:, half[c]], ALU.add).then_inc(s_npre, 1)
                dve.wait_ge(s_z, t + 1)
                dve.tensor_tensor(zh[:, :], z[:, :], h[:, :], ALU.mult).then_inc(s_zh, 1)
                dve.wait_ge(s_u, t + 1)
                for c in range(HALVES):
                    dve.wait_ge(s_n, HALVES * t + c + 1)
                    dve.tensor_tensor(un[:, half[c]], u[:, half[c]], n[:, half[c]], ALU.mult).then_inc(s_un, 1)
                dve.wait_ge(s_zh, t + 1)
                for c in range(HALVES):
                    dve.wait_ge(s_un, HALVES * t + c + 1)
                    dve.tensor_tensor(h[:, half[c]], un[:, half[c]], zh[:, half[c]], ALU.add).then_inc(s_h, 1)
                for c in range(HALVES):
                    dve.wait_ge(s_h, HALVES * t + c + 1)
                    dve.transpose(hT[:, c, (s + 1) % RING, :], h[:, half[c]]).then_inc(s_hT, 1)

            def prepare_w_out(t):
                flat = lambda a: a.rearrange("p q c o -> p (q c o)")
                if t == 0:
                    dve.wait_ge(s_wo, 16 * BLOCKS)
                    dve.transpose(flat(wt), wo[:, :, :].rearrange("p q e -> p (q e)")).then_inc(s_wt, 1)
                if t == 1:
                    dve.wait_ge(s_sum, 1)
                    dve.tensor_scalar(scale[:, :], ps_sum, 1.0 / (D * D), None, ALU.mult).then_inc(s_wt, 1)
                    dve.wait_ge(s_wt, 2)
                    dve.tensor_scalar(above[:, :], scale[:, :], EPS, 0.5, ALU.add, ALU.mult).then_inc(s_wt, 1)
                    dve.wait_ge(s_wt, 3)
                    dve.tensor_scalar(below[:, :], above[:, :], -1.0, None, ALU.mult).then_inc(s_wt, 1)
                    dve.wait_ge(s_wt, 4)
                    dve.tensor_scalar(flat(w_pos), flat(wt), above[:, :], scale[:, :], ALU.is_gt, ALU.mult).then_inc(s_wt, 1)
                if t == 2:
                    dve.tensor_scalar(flat(w_neg), flat(wt), below[:, :], scale[:, :], ALU.is_lt, ALU.mult).then_inc(s_wt, 1)
                    dve.wait_ge(s_wt, 6)
                    dve.tensor_tensor(flat(w_pos), flat(w_pos), flat(w_neg), ALU.subtract).then_inc(s_wt, 1)
                if t == 3:
                    dve.wait_ge(s_wt, 7)
                    dve.tensor_tensor(flat(w_neg), flat(w_pos), flat(wt), ALU.subtract).then_inc(s_wt, 1)
                    dve.wait_ge(s_wt, 8)
                    dve.tensor_tensor(flat(wt), flat(wt), flat(w_neg), ALU.add).then_inc(s_wt, 1)

            dve.memset(zeros[:, :], 0.0).then_inc(s_const, 1)
            dve.memset(ones[:, :], 1.0).then_inc(s_const, 1)
            dve.wait_ge(s_h0, 16)
            for c in range(HALVES):
                dve.transpose(hT[:, c, 0, :], h[:, c * HW:(c + 1) * HW]).then_inc(s_hT, 1)
            dve.wait_ge(s_x[0], 16 * BLOCKS)
            for t in range(2):
                transpose_x(t)
            dve.wait_ge(s_bias, 16 * 6)
            dve.tensor_tensor(gate_bias[:, 0:3:2, :], gate_bias[:, 0:3:2, :], bias_hh[:, :, :], ALU.add).then_inc(s_gbias, 1)
            for t in range(RING):
                if t < GROUP:
                    prepare_w_out(t)
                step(t, t, 0)
            with dve.Fori(1, LOOPS + 1) as i:
                for k in range(RING):
                    step(RING * i + k, k, i)
            for t in range(T - RING, T):
                step(t, t % RING, t // RING)
            for g in range(GROUPS - 2, GROUPS):
                read_out(g, g // 2, g % 2)


_INS = ["x", "cond_2048", "L0_cond_W_ih", "L0_cond_W_hh", "L0_cond_b_ih", "L0_cond_b_hh", "L0_ffn_weight", "L0_ffn_bias"]


def kernel(**inputs):
    import concourse.bacc as bacc
    import numpy as np
    from concourse.bass_utils import run_bass_kernel_spmd

    nc = bacc.Bacc("TRN2", target_bir_lowering=False, num_devices=1)
    arrays, args = {}, []
    for name in _INS:
        a = np.ascontiguousarray(inputs[name])
        arrays[f"in_{name}"] = a
        args.append(nc.dram_tensor(f"in_{name}", a.shape, mybir.dt.from_np(a.dtype), kind="ExternalInput").ap())
    y = nc.dram_tensor("out_y", (B, T, D), F32, kind="ExternalOutput").ap()
    gru_projection_kernel(nc, *args, y)
    return run_bass_kernel_spmd(nc, [arrays], core_ids=[0]).results[0]["out_y"]
```

```python
from contextlib import ExitStack

import concourse.bass as bass
from concourse import mybir

F32 = mybir.dt.float32
ALU = mybir.AluOpType
ACT = mybir.ActivationFunctionType

P = 128
B, T, D = 32, 32, 256
BLOCKS = P // B
BW = D // BLOCKS
HALVES = 2
HW = BW // HALVES
GATES = 3
GROUP = BLOCKS
GROUPS = T // GROUP
RING = 2 * GROUP
LOOPS = T // RING - 2
EPS = 1e-10
WARM_UP = 6, 0


def gru_projection_kernel(nc, xT, x_rows, h0, w_ih, w_hh, gate_biases, w_out, b_out, y_rows):
    with ExitStack() as ctx:
        def sb(name, shape):
            return ctx.enter_context(nc.sbuf_tensor(name, shape, F32))

        def pb(name, width):
            return ctx.enter_context(nc.psum_tensor(name, [P, 512], F32))[:, 0:width]

        def sem(name):
            return ctx.enter_context(nc.semaphore(name))

        wi = sb("wi", [P, HALVES, BLOCKS, GATES * BW])
        wh = sb("wh", [P, HALVES, BLOCKS, GATES * BW])
        wt = sb("wt", [P, HALVES, D])
        w_pos = sb("w_pos", [P, HALVES, D])
        w_neg = sb("w_neg", [P, HALVES, D])
        w_abs = sb("w_abs", [P, HALVES, D])
        x_in = sb("x_in", [P, RING, HALVES, B])
        x_res = sb("x_res", [P, 2, D])
        y = sb("y", [P, 2, D])
        h_init = sb("h_init", [P, 2, BW])
        factors = sb("factors", [P, BW, 2])
        addends = sb("addends", [P, BW, 2])
        states = sb("states", [P, BW, 2])
        hT = sb("hT", [P, HALVES, RING, B])
        biases = sb("biases", [P, 6, BW])
        gate_bias = sb("gate_bias", [P, GATES, BW])
        inputs = sb("inputs", [P, 2, 4, BW])
        out_bias = sb("out_bias", [P, D])
        zeros = sb("zeros", [P, D])
        ones = sb("ones", [P, P])
        r = sb("r", [P, BW])
        z = sb("z", [P, BW])
        rhn = sb("rhn", [P, BW])
        n_pre = sb("n_pre", [P, BW])
        abs_sum = sb("abs_sum", [P, 1])
        scale = sb("scale", [P, 1])
        above = sb("above", [P, 1])
        below = sb("below", [P, 1])
        minus_scale = sb("minus_scale", [P, 1])
        table = sb("table", [P, 1])

        ps_rh = [pb(f"ps_rh{i}", 2 * BW) for i in range(2)]
        ps_z = [pb(f"ps_z{i}", BW) for i in range(2)]
        ps_in = pb("ps_in", GATES * BW)
        ps_y = [pb(f"ps_y{i}", D) for i in range(2)]
        ps_sum = pb("ps_sum", 1)

        s_x = [sem(f"s_x{i}") for i in range(2)]
        s_res = [sem(f"s_res{i}") for i in range(2)]
        s_wi = sem("s_wi")
        s_wh = sem("s_wh")
        s_wo = sem("s_wo")
        s_h0 = sem("s_h0")
        s_bias = sem("s_bias")
        s_obias = sem("s_obias")
        s_stored = sem("s_stored")
        s_const = sem("s_const")
        s_flags = sem("s_flags")
        s_gbias = sem("s_gbias")
        s_gi = sem("s_gi")
        s_inputs = sem("s_inputs")
        s_seedz = sem("s_seedz")
        s_seedrh = sem("s_seedrh")
        s_yseed = sem("s_yseed")
        s_rh = sem("s_rh")
        s_zp = sem("s_zp")
        s_r = sem("s_r")
        s_u = sem("s_u")
        s_n = sem("s_n")
        s_rhn = sem("s_rhn")
        s_npre = sem("s_npre")
        s_zh = sem("s_zh")
        s_h = sem("s_h")
        s_hT = sem("s_hT")
        s_yp = sem("s_yp")
        s_y = sem("s_y")
        s_wt = sem("s_wt")
        s_abs = sem("s_abs")
        s_sum = sem("s_sum")

        block = ctx.enter_context(nc.Block())

        def known_below(t, bound):
            return isinstance(t, int) and t < bound

        @block.sync
        def _(sp):
            def load_x(g, slot):
                sp.dma_start(x_in[:, slot * GROUP:(slot + 1) * GROUP, :, :].rearrange("p t c b -> p (t c b)"),
                             xT[:, bass.ds(g * GROUP * BW, GROUP * BW)]).then_inc(s_x[slot], 16)

            def load_residual(g, slot):
                sp.dma_start(x_res[:, slot, :], x_rows[bass.ds(g * P, P), :]).then_inc(s_res[slot], 16)

            def store(g, slot):
                sp.dma_start(y_rows[bass.ds(g * P, P), :], y[:, slot, :]).then_inc(s_stored, 16)

            load_x(0, 0)
            for c in range(HALVES):
                sp.dma_start(wi[:, c].rearrange("p j n -> p (j n)"), w_ih[:, c, :]).then_inc(s_wi, 16)
            for c in range(HALVES):
                sp.dma_start(wh[:, c].rearrange("p j n -> p (j n)"), w_hh[:, c, :]).then_inc(s_wh, 16)
            load_x(1, 1)

            def period(g, slot, first=False, last=False):
                if not first:
                    sp.wait_ge(s_y, g - 1)
                    store(g - 2, slot)
                if not last:
                    sp.wait_ge(s_gi, (g + 1) * GROUP)
                    load_x(g + 2, slot)
                if not first:
                    sp.wait_ge(s_stored, 16 * (g - 1))
                load_residual(g, slot)

            for g in range(2):
                period(g, g, first=True)
            with sp.Fori(1, GROUPS // 2 - 1) as i:
                for slot in range(2):
                    period(2 * i + slot, slot)
            for g in range(GROUPS - 2, GROUPS):
                period(g, g % 2, last=True)
            for g in range(GROUPS - 2, GROUPS):
                sp.wait_ge(s_y, g + 1)
                store(g, g % 2)
            sp.wait_ge(s_stored, 16 * GROUPS)

        @block.gpsimd
        def _(pool):
            pool.dma_start(wt[:, :, :], w_out).then_inc(s_wo, 16)
            pool.dma_start(out_bias[:, :], b_out.to_broadcast([P, D])).then_inc(s_obias, 16)

        @block.scalar
        def _(act):
            act.dma_start(biases[:, :, :].rearrange("p g e -> p (g e)"),
                          gate_biases.to_broadcast([BLOCKS, B, 6 * BW])).then_inc(s_bias, 16)
            act.dma_start(h_init[:, :, :], h0).then_inc(s_h0, 16)
            act.wait_ge(s_const, 1)
            act.activation(table[:, :], zeros[:, 0:1], ACT.Sigmoid)

            def seed_z(s):
                act.activation(ps_z[s % 2], inputs[:, s % 2, 2, :], ACT.Copy).then_inc(s_seedz, 1)

            def seed_rh(s):
                act.activation(ps_rh[s % 2], inputs[:, s % 2, 0:2, :].rearrange("p g e -> p (g e)"),
                               ACT.Copy).then_inc(s_seedrh, 1)

            def seed_y(slot):
                act.activation(ps_y[slot], out_bias[:, :], ACT.Copy).then_inc(s_yseed, 1)

            def step(t, s):
                seeds = not (isinstance(t, int) and t == T - 1)
                if s % GROUP == 0 and not known_below(t, GROUP):
                    if known_below(t, RING):
                        act.wait_ge(s_obias, 16)
                    seed_y((s // GROUP + 1) % 2)
                if seeds:
                    act.wait_ge(s_inputs, t + 2)
                    if not known_below(t, 1):
                        act.wait_ge(s_u, t)
                    seed_z(s + 1)
                act.wait_ge(s_rh, t + 1)
                act.activation(r[:, :], ps_rh[s % 2][:, BW:2 * BW], ACT.Sigmoid).then_inc(s_r, 1)
                if seeds:
                    seed_rh(s + 1)
                act.wait_ge(s_zp, t + 1)
                act.activation(z[:, :], ps_z[s % 2], ACT.Sigmoid)
                act.activation(factors[:, :, 1], ps_z[s % 2], ACT.Sigmoid, scale=-1.0).then_inc(s_u, 1)
                for c in range(HALVES):
                    act.wait_ge(s_npre, HALVES * t + c + 1)
                    act.activation(addends[:, c * HW:(c + 1) * HW, 0], n_pre[:, c * HW:(c + 1) * HW],
                                   ACT.Tanh).then_inc(s_n, 1)

            act.wait_ge(s_wo, 16)
            act.activation(w_abs[:, :, :], wt[:, :, :], ACT.Abs, accum_out=abs_sum[:, :]).then_inc(s_abs, 1)
            act.wait_ge(s_flags, 1)
            act.wait_ge(s_inputs, 1)
            seed_z(0)
            seed_rh(0)
            for t in range(RING):
                step(t, t)
            with act.Fori(1, LOOPS + 1) as i:
                for k in range(RING):
                    step(RING * i + k, k)
            for t in range(T - RING, T):
                step(t, t % RING)
            seed_y((GROUPS - 1) % 2)

        @block.tensor
        def _(pe):
            def tiles(bank, stationary, w, c0, c1, start=False, stop=True, seeded=True):
                for j in range(BLOCKS):
                    done = pe.matmul(bank[j * B:(j + 1) * B, :], stationary, w[:, j, c0:c1],
                                     start=start, stop=stop, tile_position=(0, j * B), skip_group_check=seeded)
                return done

            def input_product(t, s, rounds):
                if s % GROUP == 0:
                    pe.wait_ge(s_x[s // GROUP % 2], 16 * (rounds + 1))
                if not known_below(t, 1):
                    pe.wait_ge(s_inputs, t)
                for c in range(HALVES):
                    done = tiles(ps_in, x_in[:, s % RING, c, :], wi[:, c], 0, GATES * BW,
                                 start=c == 0, stop=c == 1, seeded=False)
                done.then_inc(s_gi, 1)

            def hidden_product(t, s):
                for c in range(HALVES):
                    pe.wait_ge(s_hT, HALVES * t + c + 1)
                    if c == 0:
                        pe.wait_ge(s_seedrh, t + 1)
                    done = tiles(ps_rh[s % 2], hT[:, c, s % RING, :], wh[:, c], 0, 2 * BW)
                done.then_inc(s_rh, 1)
                pe.wait_ge(s_seedz, t + 1)
                for c in range(HALVES):
                    done = tiles(ps_z[s % 2], hT[:, c, s % RING, :], wh[:, c], 2 * BW, 3 * BW)
                done.then_inc(s_zp, 1)

            def project(slot, c, half):
                cols = slice(half * D // 2, (half + 1) * D // 2)
                for q in range(GROUP):
                    done = pe.matmul(ps_y[slot][q * B:(q + 1) * B, cols], hT[:, c, (slot * GROUP + q + 1) % RING, :],
                                     wt[:, c, cols], start=False, stop=True, tile_position=(0, q * B),
                                     skip_group_check=True)
                return done

            def step(t, s, rounds):
                hidden_product(t, s)
                if not (isinstance(t, int) and t >= T - 2):
                    input_product(t + 2, (s + 2) % RING, rounds + (s + 2) // RING)
                if not known_below(t, GROUP):
                    piece = s % GROUP
                    if piece == 0:
                        pe.wait_ge(s_yseed, 2 * rounds + s // GROUP)
                        if isinstance(t, int) and t == GROUP:
                            pe.wait_ge(s_wt, 8)
                    done = project((s // GROUP + 1) % 2, piece % HALVES, piece // HALVES)
                    if piece == GROUP - 1:
                        done.then_inc(s_yp, 1)

            pe.wait_ge(s_const, 1)
            for bank in ps_rh + ps_z + ps_y:
                for j in range(BLOCKS):
                    done = pe.matmul(bank[j * B:(j + 1) * B, :], zeros[:, 0:B], zeros[:, 0:bank.shape[1]],
                                     start=True, stop=True, tile_position=(0, j * B))
            done.then_inc(s_flags, 1)

            def keep_warm(times):
                for _ in range(times):
                    pe.matmul(ps_in[:, 0:P], zeros[:, 0:P], zeros[:, 0:P], start=True, stop=True)

            pe.wait_ge(s_const, 2)
            pe.wait_ge(s_abs, 1)
            pe.matmul(ps_sum, ones[:, :], abs_sum[:, :], start=True, stop=True).then_inc(s_sum, 1)
            keep_warm(WARM_UP[0])
            pe.wait_ge(s_wi, 16 * HALVES)
            input_product(0, 0, 0)
            keep_warm(WARM_UP[1])
            input_product(1, 1, 0)
            pe.wait_ge(s_wh, 16 * HALVES)
            for t in range(RING):
                step(t, t, 0)
            with pe.Fori(1, LOOPS + 1) as i:
                for k in range(RING):
                    step(RING * i + k, k, i)
            for t in range(T - RING, T):
                step(t, t % RING, t // RING)
            pe.wait_ge(s_yseed, GROUPS)
            for c in range(HALVES):
                pe.wait_ge(s_hT, HALVES * T + c + 1)
                for half in range(2):
                    done = project((GROUPS - 1) % 2, c, half)
            done.then_inc(s_yp, 1)

        @block.vector
        def _(dve):
            halves = [slice(c * HW, (c + 1) * HW) for c in range(HALVES)]

            def take_inputs(t, s):
                dve.wait_ge(s_gi, t + 1)
                if not known_below(t, 2):
                    dve.wait_ge(s_seedrh, t - 1)
                dve.tensor_tensor(inputs[:, s % 2, 1:4, :].rearrange("p g e -> p (g e)"), ps_in,
                                  gate_bias[:, :, :].rearrange("p g e -> p (g e)"), ALU.add).then_inc(s_inputs, 1)

            def read_out(g, rounds, slot):
                dve.wait_ge(s_yp, g + 1)
                dve.wait_ge(s_res[slot], 16 * (rounds + 1))
                dve.tensor_tensor(y[:, slot, :], ps_y[slot], x_res[:, slot, :], ALU.add).then_inc(s_y, 1)

            def step(t, s, rounds):
                if not (isinstance(t, int) and t == T - 1):
                    take_inputs(t + 1, s + 1)
                if s % GROUP == 0 and not known_below(t, RING):
                    read_out(2 * rounds + s // GROUP - 2, rounds - 1, s // GROUP)
                dve.wait_ge(s_r, t + 1)
                for c, half in enumerate(halves):
                    dve.tensor_tensor(rhn[:, half], ps_rh[s % 2][:, half], r[:, half], ALU.mult).then_inc(s_rhn, 1)
                for c, half in enumerate(halves):
                    dve.wait_ge(s_rhn, HALVES * t + c + 1)
                    dve.tensor_tensor(n_pre[:, half], inputs[:, s % 2, 3, half], rhn[:, half], ALU.add).then_inc(s_npre, 1)
                dve.wait_ge(s_u, t + 1)
                old = h_init[:, 0, :] if known_below(t, 1) else states[:, :, 1]
                dve.tensor_tensor(addends[:, :, 1], z[:, :], old, ALU.mult).then_inc(s_zh, 1)
                for c, half in enumerate(halves):
                    dve.wait_ge(s_n, HALVES * t + c + 1)
                    if c == 0:
                        dve.wait_ge(s_zh, t + 1)
                    pairs = [a[:, half, :].rearrange("p e k -> p (e k)") for a in (states, factors, addends)]
                    dve.tensor_tensor_scan(*pairs, 0.0, ALU.mult, ALU.add).then_inc(s_h, 1)
                for c, half in enumerate(halves):
                    dve.wait_ge(s_h, HALVES * t + c + 1)
                    dve.transpose(hT[:, c, (s + 1) % RING, :], states[:, half, 1]).then_inc(s_hT, 1)

            def prepare_w_out():
                dve.wait_ge(s_sum, 1)
                dve.tensor_scalar(scale[:, :], ps_sum[:, 0:1], 1.0 / (D * D), None, ALU.mult).then_inc(s_wt, 1)
                dve.wait_ge(s_wt, 1)
                dve.tensor_scalar(above[:, :], scale[:, :], EPS, 0.5, ALU.add, ALU.mult).then_inc(s_wt, 1)
                dve.tensor_scalar(minus_scale[:, :], scale[:, :], -1.0, None, ALU.mult).then_inc(s_wt, 1)
                dve.wait_ge(s_wt, 2)
                dve.tensor_scalar(below[:, :], above[:, :], -1.0, None, ALU.mult).then_inc(s_wt, 1)
                flat, pos, neg = (a[:, :, :].rearrange("p c o -> p (c o)") for a in (wt, w_pos, w_neg))
                dve.tensor_scalar(pos, flat, above[:, :], None, ALU.is_gt).then_inc(s_wt, 1)
                dve.wait_ge(s_wt, 5)
                dve.scalar_tensor_tensor(neg, flat, below[:, :], pos, ALU.is_lt, ALU.subtract).then_inc(s_wt, 1)
                dve.wait_ge(s_wt, 6)
                dve.scalar_tensor_tensor(pos, neg, minus_scale[:, :], flat, ALU.mult, ALU.subtract).then_inc(s_wt, 1)
                dve.wait_ge(s_wt, 7)
                dve.tensor_tensor(flat, flat, pos, ALU.add).then_inc(s_wt, 1)

            dve.memset(zeros[:, :], 0.0).then_inc(s_const, 1)
            dve.memset(ones[:, :], 1.0).then_inc(s_const, 1)
            dve.memset(factors[:, :, 0], 0.0).then_inc(s_const, 1)
            dve.wait_ge(s_bias, 16)
            dve.tensor_tensor(gate_bias[:, 0:2, :], biases[:, 0:2, :], biases[:, 3:5, :], ALU.add).then_inc(s_gbias, 1)
            dve.tensor_copy(gate_bias[:, 2, :], biases[:, 2, :]).then_inc(s_gbias, 1)
            for i in range(2):
                dve.tensor_copy(inputs[:, i, 0, :], biases[:, 5, :]).then_inc(s_gbias, 1)
            dve.wait_ge(s_h0, 16)
            for c in range(HALVES):
                dve.tensor_copy(hT[:, c, 0, :], h_init[:, 1, c * B:(c + 1) * B]).then_inc(s_hT, 1)
            prepare_w_out()
            dve.wait_ge(s_gbias, 4)
            take_inputs(0, 0)
            for t in range(RING):
                step(t, t, 0)
            with dve.Fori(1, LOOPS + 1) as i:
                for k in range(RING):
                    step(RING * i + k, k, i)
            for t in range(T - RING, T):
                step(t, t % RING, t // RING)
            for g in range(GROUPS - 2, GROUPS):
                read_out(g, g // 2, g % 2)




def _transposed(rows):
    rows = rows.reshape(BLOCKS, HALVES, HW, *rows.shape[1:])
    return rows.transpose(0, 2, 1, *range(3, rows.ndim)).reshape(P, HALVES, *rows.shape[3:])


def _by_block(w, order):
    w = w.reshape(*w.shape[:-1], GATES, BLOCKS, BW)[..., order, :, :]
    return w.swapaxes(-3, -2).reshape(*w.shape[:-3], GATES * D)


def kernel(x, cond_2048, L0_cond_W_ih, L0_cond_W_hh, L0_cond_b_ih, L0_cond_b_hh, L0_ffn_weight, L0_ffn_bias):
    import concourse.bacc as bacc
    import numpy as np
    from concourse.bass_utils import run_bass_kernel_spmd

    x, h0, w_ih, w_hh, b_ih, b_hh, w_out, b_out = (
        np.asarray(a) for a in (x, cond_2048, L0_cond_W_ih, L0_cond_W_hh, L0_cond_b_ih, L0_cond_b_hh,
                                L0_ffn_weight, L0_ffn_bias))
    r, z, n = range(GATES)
    packed_h0 = h0.reshape(B, BLOCKS, BW).swapaxes(0, 1).reshape(P, 1, BW)
    transposed_h0 = _transposed(h0.T).reshape(P, 1, BW)
    laid_out = {
        "xT": _transposed(x.transpose(2, 1, 0)).swapaxes(1, 2).reshape(P, T * BW),
        "x_rows": x.swapaxes(0, 1).reshape(T * B, D),
        "h0": np.concatenate([packed_h0, transposed_h0], axis=1),
        "w_ih": _by_block(_transposed(w_ih), [r, z, n]),
        "w_hh": _by_block(_transposed(w_hh), [n, r, z]),
        "gate_biases": np.concatenate([_by_block(b, [r, z, n]).reshape(BLOCKS, 1, GATES * BW) for b in (b_ih, b_hh)], axis=2),
        "w_out": _transposed(w_out.T),
        "b_out": b_out.reshape(1, D),
    }
    nc = bacc.Bacc("TRN2", target_bir_lowering=False, num_devices=1)
    arrays, args = {}, []
    for name, a in laid_out.items():
        arrays[name] = np.ascontiguousarray(a)
        args.append(nc.dram_tensor(name, a.shape, mybir.dt.from_np(a.dtype), kind="ExternalInput").ap())
    y_rows = nc.dram_tensor("y_rows", (T * B, D), F32, kind="ExternalOutput").ap()
    gru_projection_kernel(nc, *args, y_rows)
    got = run_bass_kernel_spmd(nc, [arrays], core_ids=[0]).results[0]["y_rows"]
    return np.ascontiguousarray(np.asarray(got).reshape(T, B, D).swapaxes(0, 1))
```

```python
from contextlib import ExitStack

import concourse.bass as bass
from concourse import mybir

F32 = mybir.dt.float32
ALU = mybir.AluOpType
ACT = mybir.ActivationFunctionType

P = 128
B, T, D = 32, 32, 256
BLOCKS = P // B
BW = D // BLOCKS
HALVES = 2
HW = BW // HALVES
GATES = 3
GROUP = BLOCKS
GROUPS = T // GROUP
RING = 2 * GROUP
LOOPS = T // RING - 2
EPS = 1e-10
LAST = GROUPS - 1
FLAG_STEPS = 0, 2
SIDES = 3
PREPARE = 2


def gru_projection_kernel(nc, xT, x_rows, h0, w_ih, w_hh, w_hz, gate_biases, w_out, b_out, y_rows):
    with ExitStack() as ctx:
        def sb(name, shape):
            return ctx.enter_context(nc.sbuf_tensor(name, shape, F32))

        def pb(name, width):
            return ctx.enter_context(nc.psum_tensor(name, [P, 512], F32))[:, 0:width]

        def sem(name):
            return ctx.enter_context(nc.semaphore(name))

        wi = sb("wi", [P, HALVES, BLOCKS, GATES * BW])
        wh = sb("wh", [P, HALVES, BLOCKS, 2 * BW])
        wh_z = sb("wh_z", [P, HALVES, BLOCKS, BW])
        wt = sb("wt", [P, HALVES, D])
        w_above = sb("w_above", [P, HALVES, D])
        w_ternary = sb("w_ternary", [P, HALVES, D])
        w_delta = sb("w_delta", [P, HALVES, D])
        w_abs = sb("w_abs", [P, HALVES, D])
        x_in = sb("x_in", [P, RING, HALVES, B])
        x_res = sb("x_res", [P, 2, D])
        y = sb("y", [P, 2, D])
        last_x = sb("last_x", [P, BW])
        last_bias = sb("last_bias", [P, BW])
        last_res = sb("last_res", [P, BW])
        last_y = sb("last_y", [P, BW])
        h_init = sb("h_init", [P, BW])
        factors = sb("factors", [P, BW, 3])
        addends = sb("addends", [P, BW, 3])
        states = sb("states", [P, BW, 3])
        hT = sb("hT", [P, HALVES, RING, B])
        biases = sb("biases", [P, 2, GATES, BW])
        gate_bias = sb("gate_bias", [P, GATES, BW])
        inputs = sb("inputs", [P, 2, GATES, BW, 2])
        out_bias = sb("out_bias", [P, D])
        zeros = sb("zeros", [P, D])
        ones = sb("ones", [P, P])
        r = sb("r", [P, BW, 2])
        n_pre = sb("n_pre", [P, BW, 2])
        abs_sum = sb("abs_sum", [P, 1])
        above = sb("above", [P, 1])
        below = sb("below", [P, 1])
        minus_scale = sb("minus_scale", [P, 1])
        table = sb("table", [P, 1])

        ps_rh = [pb(f"ps_rh{i}", 2 * BW * 2) for i in range(2)]
        ps_z = [pb(f"ps_z{i}", BW) for i in range(2)]
        ps_in = pb("ps_in", GATES * BW)
        ps_y = [pb(f"ps_y{i}", D) for i in range(2)]
        ps_once = pb("ps_once", GATES * BW)

        s_x = [sem(f"s_x{i}") for i in range(2)]
        s_res = [sem(f"s_res{i}") for i in range(2)]
        s_wi = [sem(f"s_wi{c}") for c in range(HALVES)]
        s_wh = [sem(f"s_wh{c}") for c in range(HALVES)]
        s_wz = sem("s_wz")
        s_wo = sem("s_wo")
        s_h0 = sem("s_h0")
        s_bias = sem("s_bias")
        s_obias = sem("s_obias")
        s_last_in = sem("s_last_in")
        s_last_res = sem("s_last_res")
        s_last_y = sem("s_last_y")
        s_stored = sem("s_stored")
        s_const = sem("s_const")
        s_flags = sem("s_flags")
        s_gbias = sem("s_gbias")
        s_gi = sem("s_gi")
        s_inputs = sem("s_inputs")
        s_seedz = sem("s_seedz")
        s_seedrh = sem("s_seedrh")
        s_yseed = sem("s_yseed")
        s_rh = sem("s_rh")
        s_zp = sem("s_zp")
        s_r = sem("s_r")
        s_u = sem("s_u")
        s_n = sem("s_n")
        s_npre = sem("s_npre")
        s_h = sem("s_h")
        s_hT = sem("s_hT")
        s_yp = sem("s_yp")
        s_y = sem("s_y")
        s_wt = sem("s_wt")
        s_abs = sem("s_abs")
        s_sum = sem("s_sum")

        block = ctx.enter_context(nc.Block())

        def peeled(t, *steps):
            return isinstance(t, int) and t in steps

        def known_below(t, bound):
            return isinstance(t, int) and t < bound

        def input_bank(t):
            return ps_once if peeled(t, 1) else ps_in

        @block.sync
        def _(sp):
            def packed(rows):
                return rows.rearrange("b (j e) -> j b e", j=BLOCKS)

            def load_x(g, slot):
                sp.dma_start(x_in[:, slot * GROUP:(slot + 1) * GROUP, :, :].rearrange("p t c b -> p (t c b)"),
                             xT[:, bass.ds(g * GROUP * BW, GROUP * BW)]).then_inc(s_x[slot], 16)

            def load_residual(g, slot):
                sp.dma_start(x_res[:, slot, :], x_rows[bass.ds(g * P, P), :]).then_inc(s_res[slot], 16)

            def store(g, slot):
                sp.dma_start(y_rows[bass.ds(g * P, P), :], y[:, slot, :]).then_inc(s_stored, 16)

            load_x(0, 0)
            for c in range(HALVES):
                sp.dma_start(wi[:, c].rearrange("p j n -> p (j n)"), w_ih[:, c, :]).then_inc(s_wi[c], 16)
            sp.dma_start(biases[:, :, :, :].rearrange("p i g e -> p (i g e)"),
                         gate_biases.to_broadcast([BLOCKS, B, 2 * GATES * BW])).then_inc(s_bias, 16)
            sp.dma_start(h_init[:, :], h0).then_inc(s_h0, 16)
            for c in range(HALVES):
                sp.dma_start(wh[:, c].rearrange("p j n -> p (j n)"), w_hh[:, c, :]).then_inc(s_wh[c], 16)
            sp.dma_start(wh_z[:, :].rearrange("p c j n -> p c (j n)"), w_hz).then_inc(s_wz, 16)
            sp.dma_start(wt[:, :, :], w_out).then_inc(s_wo, 16)
            load_x(1, 1)
            sp.dma_start(out_bias[:, :], b_out.to_broadcast([P, D])).then_inc(s_obias, 16)

            def period(g, slot, first=False, last=False):
                if not first:
                    sp.wait_ge(s_y, g - 1)
                    store(g - 2, slot)
                if not last:
                    sp.wait_ge(s_gi, (g + 1) * GROUP)
                    load_x(g + 2, slot)
                if not first:
                    sp.wait_ge(s_stored, 16 * (g - 1))
                load_residual(g, slot)

            for g in range(2):
                period(g, g, first=True)
            sp.dma_start(last_x[:, :], packed(x_rows[T * B - B:, :])).then_inc(s_last_in, 16)
            sp.dma_start(last_bias[:, :], b_out.rearrange("a (j e) -> j a e", j=BLOCKS)
                         .to_broadcast([BLOCKS, B, BW])).then_inc(s_last_in, 16)
            with sp.Fori(1, GROUPS // 2 - 1) as i:
                for slot in range(2):
                    period(2 * i + slot, slot)
            for g in range(GROUPS - 2, GROUPS):
                period(g, g % 2, last=True)
            sp.wait_ge(s_y, LAST)
            store(LAST - 1, (LAST - 1) % 2)
            sp.wait_ge(s_y, LAST + 1)
            sp.dma_start(y_rows[LAST * P:T * B - B, :], y[0:P - B, LAST % 2, :]).then_inc(s_stored, 16)
            sp.wait_ge(s_y, LAST + 2)
            sp.dma_start(packed(y_rows[T * B - B:, :]), last_y[:, :]).then_inc(s_stored, 16)
            sp.wait_ge(s_stored, 16 * (GROUPS + 1))

        @block.scalar
        def _(act):
            act.wait_ge(s_const, 1)
            act.activation(table[:, :], zeros[:, 0:1], ACT.Sigmoid)

            def seed_z(s):
                act.activation(ps_z[s % 2], inputs[:, s % 2, 2, :, 1], ACT.Copy).then_inc(s_seedz, 1)

            def seed_r(s):
                act.activation(ps_rh[s % 2][:, 2 * BW::2], inputs[:, s % 2, 1, :, 1], ACT.Copy)

            def seed_n(s):
                act.activation(ps_rh[s % 2][:, 0:2 * BW], inputs[:, s % 2, 0, :, :].rearrange("p e k -> p (e k)"),
                               ACT.Copy).then_inc(s_seedrh, 1)

            def seed_y(slot):
                act.activation(ps_y[slot], out_bias[:, :], ACT.Copy).then_inc(s_yseed, 1)

            def step(t, s):
                seeds = not peeled(t, T - 1)
                if s % GROUP == 0 and not known_below(t, GROUP):
                    if known_below(t, RING):
                        act.wait_ge(s_obias, 16)
                        act.wait_ge(s_flags, 5 + len(FLAG_STEPS))
                    seed_y((s // GROUP + 1) % 2)
                if peeled(t, T - 1):
                    seed_y(LAST % 2)
                if known_below(t, 1):
                    act.wait_ge(s_h0, 16)
                    old = h_init[:, :]
                else:
                    act.wait_ge(s_h, HALVES * t)
                    old = states[:, :, 2]
                act.activation(addends[:, :, ::2], old.rearrange("p (e k) -> p e k", k=1).to_broadcast([P, BW, 2]),
                               ACT.Copy)
                if seeds:
                    act.wait_ge(s_inputs, t + 2)
                    if not known_below(t, 1):
                        act.wait_ge(s_u, t)
                    seed_z(s + 1)
                    seed_r(s + 1)
                act.wait_ge(s_rh, t + 1)
                act.activation(r[:, :, 1], ps_rh[s % 2][:, 2 * BW::2], ACT.Sigmoid).then_inc(s_r, 1)
                if seeds:
                    seed_n(s + 1)
                act.wait_ge(s_zp, t + 1)
                act.activation(factors[:, :, 2], ps_z[s % 2], ACT.Sigmoid, scale=-1.0).then_inc(s_u, 1)
                for c in range(HALVES):
                    act.wait_ge(s_npre, HALVES * t + c + 1)
                    act.activation(addends[:, c * HW:(c + 1) * HW, 1], n_pre[:, c * HW:(c + 1) * HW, 1],
                                   ACT.Tanh).then_inc(s_n, 1)
                if known_below(t, 1):
                    act.wait_ge(s_wo, 16)
                    act.activation(w_abs[:, :, :], wt[:, :, :], ACT.Abs, accum_out=abs_sum[:, :]).then_inc(s_abs, 1)

            act.wait_ge(s_flags, 4)
            act.wait_ge(s_inputs, 1)
            seed_r(0)
            seed_n(0)
            seed_z(0)
            for t in range(RING):
                step(t, t)
            with act.Fori(1, LOOPS + 1) as i:
                for k in range(RING):
                    step(RING * i + k, k)
            for t in range(T - RING, T):
                step(t, t % RING)

        @block.tensor
        def _(pe):
            def tiles(bank, stationary, w, c0, c1, start=False, stop=True, seeded=True):
                for j in range(BLOCKS):
                    done = pe.matmul(bank[j * B:(j + 1) * B, :], stationary, w[:, j, c0:c1],
                                     start=start, stop=stop, tile_position=(0, j * B), skip_group_check=seeded)
                return done

            def input_product(t, s, rounds):
                if s % GROUP == 0:
                    pe.wait_ge(s_x[s // GROUP % 2], 16 * (rounds + 1))
                if not known_below(t, 2):
                    pe.wait_ge(s_inputs, t)
                for c in range(HALVES):
                    if known_below(t, 1):
                        pe.wait_ge(s_wi[c], 16)
                    done = tiles(input_bank(t), x_in[:, s % RING, c, :], wi[:, c], 0, GATES * BW,
                                 start=c == 0, stop=c == 1, seeded=False)
                done.then_inc(s_gi, 1)

            def hidden_product(t, s):
                for c in range(HALVES):
                    pe.wait_ge(s_hT, HALVES * t + c + 1)
                    if known_below(t, 1):
                        pe.wait_ge(s_wh[c], 16)
                    if c == 0:
                        pe.wait_ge(s_seedrh, t + 1)
                    done = tiles(ps_rh[s % 2][:, ::2], hT[:, c, s % RING, :], wh[:, c], 0, 2 * BW)
                done.then_inc(s_rh, 1)
                if known_below(t, 1):
                    pe.wait_ge(s_wz, 16)
                pe.wait_ge(s_seedz, t + 1)
                for c in range(HALVES):
                    done = tiles(ps_z[s % 2], hT[:, c, s % RING, :], wh_z[:, c], 0, BW)
                done.then_inc(s_zp, 1)

            def project(slot, c, half, steps=GROUP):
                cols = slice(half * D // 2, (half + 1) * D // 2)
                for q in range(steps):
                    done = pe.matmul(ps_y[slot][q * B:(q + 1) * B, cols], hT[:, c, (slot * GROUP + q + 1) % RING, :],
                                     wt[:, c, cols], start=False, stop=True, tile_position=(0, q * B),
                                     skip_group_check=True)
                return done

            def set_flags(bank, start=True):
                for j in range(BLOCKS):
                    done = pe.matmul(bank[j * B:(j + 1) * B, :], zeros[:, 0:B], zeros[:, 0:bank.shape[1]],
                                     start=start, stop=True, tile_position=(0, j * B), skip_group_check=True)
                done.then_inc(s_flags, 1)

            def step(t, s, rounds):
                hidden_product(t, s)
                if peeled(t, 1):
                    pe.wait_ge(s_abs, 1)
                    pe.matmul(ps_once[:, 0:1], ones[:, :], abs_sum[:, :], start=True, stop=True).then_inc(s_sum, 1)
                if not peeled(t, T - 2, T - 1):
                    input_product(t + 2, (s + 2) % RING, rounds + (s + 2) // RING)
                if peeled(t, *FLAG_STEPS):
                    part, width = FLAG_STEPS.index(t), D // len(FLAG_STEPS)
                    set_flags(ps_y[1][:, part * width:(part + 1) * width], start=part == 0)
                if peeled(t, T - 1):
                    pe.wait_ge(s_yseed, GROUPS)
                    for c in range(HALVES):
                        for half in range(2):
                            done = project(LAST % 2, c, half, GROUP - 1)
                    done.then_inc(s_yp, 1)
                elif not known_below(t, GROUP):
                    piece = s % GROUP
                    if piece == 0:
                        pe.wait_ge(s_yseed, 2 * rounds + s // GROUP)
                    if known_below(t, GROUP + HALVES):
                        pe.wait_ge(s_wt, SIDES + 2 * HALVES + 2 * (piece + 1))
                    pieces = (piece, piece + 1) if peeled(t, T - 2) else (piece,)
                    for piece in pieces:
                        done = project((s // GROUP + 1) % 2, piece % HALVES, piece // HALVES)
                    if pieces[-1] == GROUP - 1:
                        done.then_inc(s_yp, 1)

            pe.wait_ge(s_const, 1)
            for bank in ps_z + ps_rh + ps_y[0:1]:
                set_flags(bank)
            input_product(0, 0, 0)
            input_product(1, 1, 0)
            for t in range(RING):
                step(t, t, 0)
            with pe.Fori(1, LOOPS + 1) as i:
                for k in range(RING):
                    step(RING * i + k, k, i)
            for t in range(T - RING, T):
                step(t, t % RING, t // RING)
            for c in range(HALVES):
                pe.wait_ge(s_hT, HALVES * T + c + 1)
                done = tiles(ps_once[:, 0:BW], hT[:, c, T % RING, :], wt[:, c].rearrange("p (j e) -> p j e", j=BLOCKS),
                             0, BW, start=c == 0, stop=c == 1, seeded=False)
            done.then_inc(s_last_y, 1)

        @block.vector
        def _(dve):
            halves = [slice(c * HW, (c + 1) * HW) for c in range(HALVES)]

            def take_inputs(t, s):
                dve.wait_ge(s_gi, t + 1)
                if not known_below(t, 2):
                    dve.wait_ge(s_seedrh, t - 1)
                dve.tensor_tensor(inputs[:, s % 2, :, :, 1], input_bank(t).rearrange("p (g e) -> p g e", g=GATES),
                                  gate_bias[:, :, :], ALU.add).then_inc(s_inputs, 1)

            def read_out(g, rounds, slot):
                dve.wait_ge(s_yp, g + 1)
                dve.wait_ge(s_res[slot], 16 * (rounds + 1))
                dve.tensor_tensor(y[:, slot, :], ps_y[slot], x_res[:, slot, :], ALU.add).then_inc(s_y, 1)

            def step(t, s, rounds):
                if peeled(t, *range(PREPARE, PREPARE + 2 + HALVES)):
                    prepare_w_out(t - PREPARE)
                if peeled(t, T - 1):
                    read_out(LAST - 1, (LAST - 1) // 2, (LAST - 1) % 2)
                    dve.wait_ge(s_last_in, 32)
                    dve.tensor_tensor(last_res[:, :], last_x[:, :], last_bias[:, :], ALU.add).then_inc(s_last_res, 1)
                dve.wait_ge(s_r, t + 1)
                for c, half in enumerate(halves):
                    dve.tensor_tensor_scan(*(a[:, half, :].rearrange("p e k -> p (e k)") for a in (n_pre, r)),
                                           ps_rh[s % 2][:, c * BW:(c + 1) * BW], 0.0, ALU.mult, ALU.add).then_inc(s_npre, 1)
                for c, half in enumerate(halves):
                    dve.wait_ge(s_n, HALVES * t + c + 1)
                    triples = [a[:, half, :].rearrange("p e k -> p (e k)") for a in (states, factors, addends)]
                    dve.tensor_tensor_scan(*triples, 0.0, ALU.mult, ALU.add).then_inc(s_h, 1)
                for c, half in enumerate(halves):
                    dve.wait_ge(s_h, HALVES * t + c + 1)
                    dve.transpose(hT[:, c, (s + 1) % RING, :], states[:, half, 2]).then_inc(s_hT, 1)
                if not peeled(t, T - 2, T - 1):
                    take_inputs(t + 2, s)
                if s % GROUP == 0 and not known_below(t, RING):
                    read_out(2 * rounds + s // GROUP - 2, rounds - 1, s // GROUP)

            def prepare_w_out(part):
                if part == 0:
                    dve.wait_ge(s_sum, 1)
                    for side, factor, plus in ((above, 0.5, 0.5 * EPS), (below, -0.5, -0.5 * EPS), (minus_scale, -1.0, 0.0)):
                        dve.tensor_scalar(side[:, :], ps_once[:, 0:1], factor / (D * D), plus,
                                          ALU.mult, ALU.add).then_inc(s_wt, 1)
                    dve.wait_ge(s_wt, 1)
                    for c in range(HALVES):
                        dve.tensor_scalar(w_above[:, c], wt[:, c], above[:, :], None, ALU.is_gt).then_inc(s_wt, 1)
                elif part == 1:
                    for c in range(HALVES):
                        dve.wait_ge(s_wt, SIDES + c + 1)
                        dve.scalar_tensor_tensor(w_ternary[:, c], wt[:, c], below[:, :], w_above[:, c],
                                                 ALU.is_lt, ALU.subtract).then_inc(s_wt, 1)
                else:
                    c = part - 2
                    dve.wait_ge(s_wt, SIDES + 2 * HALVES)
                    dve.scalar_tensor_tensor(w_delta[:, c], w_ternary[:, c], minus_scale[:, :], wt[:, c],
                                             ALU.mult, ALU.subtract).then_inc(s_wt, 1)
                    dve.wait_ge(s_wt, SIDES + 2 * HALVES + 2 * c + 1)
                    dve.tensor_tensor(wt[:, c], wt[:, c], w_delta[:, c], ALU.add).then_inc(s_wt, 1)

            dve.memset(zeros[:, :], 0.0).then_inc(s_const, 1)
            dve.memset(ones[:, :], 1.0).then_inc(s_const, 1)
            dve.memset(factors[:, :, 0], 0.0).then_inc(s_const, 1)
            dve.memset(factors[:, :, 1], -1.0).then_inc(s_const, 1)
            dve.memset(r[:, :, 0], 0.0).then_inc(s_const, 1)
            dve.wait_ge(s_bias, 16)
            dve.tensor_tensor(gate_bias[:, 1:3, :], biases[:, 0, 1:3, :], biases[:, 1, 1:3, :], ALU.add).then_inc(s_gbias, 1)
            dve.tensor_copy(gate_bias[:, 0, :], biases[:, 0, 0, :]).then_inc(s_gbias, 1)
            for i in range(2):
                dve.tensor_copy(inputs[:, i, 0, :, 0], biases[:, 1, 0, :]).then_inc(s_gbias, 1)
            dve.wait_ge(s_gbias, 4)
            take_inputs(0, 0)
            dve.wait_ge(s_h0, 16)
            for c in range(HALVES):
                dve.transpose(hT[:, c, 0, :], h_init[:, halves[c]]).then_inc(s_hT, 1)
            take_inputs(1, 1)
            for t in range(RING):
                step(t, t, 0)
            with dve.Fori(1, LOOPS + 1) as i:
                for k in range(RING):
                    step(RING * i + k, k, i)
            for t in range(T - RING, T):
                step(t, t % RING, t // RING)
            early = slice(0, P - B)
            dve.wait_ge(s_yp, GROUPS)
            dve.wait_ge(s_res[LAST % 2], 16 * GROUPS // 2)
            dve.tensor_tensor(y[early, LAST % 2, :], ps_y[LAST % 2][early, :], x_res[early, LAST % 2, :],
                              ALU.add).then_inc(s_y, 1)
            dve.wait_ge(s_last_y, 1)
            dve.wait_ge(s_last_res, 1)
            dve.tensor_tensor(last_y[:, :], ps_once[:, 0:BW], last_res[:, :], ALU.add).then_inc(s_y, 1)




def _transposed(rows):
    rows = rows.reshape(BLOCKS, HALVES, HW, *rows.shape[1:])
    return rows.transpose(0, 2, 1, *range(3, rows.ndim)).reshape(P, HALVES, *rows.shape[3:])


def _by_block(w, order):
    w = w.reshape(*w.shape[:-1], GATES, BLOCKS, BW)[..., order, :, :]
    return w.swapaxes(-3, -2).reshape(*w.shape[:-3], len(order) * D)


def kernel(x, cond_2048, L0_cond_W_ih, L0_cond_W_hh, L0_cond_b_ih, L0_cond_b_hh, L0_ffn_weight, L0_ffn_bias):
    import concourse.bacc as bacc
    import numpy as np
    from concourse.bass_utils import run_bass_kernel_spmd

    x, h0, w_ih, w_hh, b_ih, b_hh, w_out, b_out = (
        np.asarray(a) for a in (x, cond_2048, L0_cond_W_ih, L0_cond_W_hh, L0_cond_b_ih, L0_cond_b_hh,
                                L0_ffn_weight, L0_ffn_bias))
    r, z, n = range(GATES)
    laid_out = {
        "xT": _transposed(x.transpose(2, 1, 0)).swapaxes(1, 2).reshape(P, T * BW),
        "x_rows": x.swapaxes(0, 1).reshape(T * B, D),
        "h0": h0.reshape(B, BLOCKS, BW).swapaxes(0, 1).reshape(P, BW),
        "w_ih": _by_block(_transposed(w_ih), [n, r, z]),
        "w_hh": _by_block(_transposed(w_hh), [n, r]),
        "w_hz": _by_block(_transposed(w_hh), [z]),
        "gate_biases": np.concatenate([_by_block(b, [n, r, z]).reshape(BLOCKS, 1, GATES * BW) for b in (b_ih, b_hh)],
                                      axis=2),
        "w_out": _transposed(w_out.T),
        "b_out": b_out.reshape(1, D),
    }
    nc = bacc.Bacc("TRN2", target_bir_lowering=False, num_devices=1)
    arrays, args = {}, []
    for name, a in laid_out.items():
        arrays[name] = np.ascontiguousarray(a)
        args.append(nc.dram_tensor(name, a.shape, mybir.dt.from_np(a.dtype), kind="ExternalInput").ap())
    y_rows = nc.dram_tensor("y_rows", (T * B, D), F32, kind="ExternalOutput").ap()
    gru_projection_kernel(nc, *args, y_rows)
    got = run_bass_kernel_spmd(nc, [arrays], core_ids=[0]).results[0]["y_rows"]
    return np.ascontiguousarray(np.asarray(got).reshape(T, B, D).swapaxes(0, 1))
```
